# Optimizing a Trainium2 kernel written in Bass

```python
import numpy as np
import jax
import jax.numpy as jnp

def _softmax(x, axis=-1):
    return jax.nn.softmax(x, axis=axis)

def _gelu(x):
    return jax.nn.gelu(x, approximate=True)

def _silu(x):
    return jax.nn.silu(x)

def _sigmoid(x):
    return jax.nn.sigmoid(x)

def _layernorm(x, axis=-1, eps=1e-05):
    m = jnp.mean(x, axis=axis, keepdims=True)
    v = jnp.var(x, axis=axis, keepdims=True)
    return (x - m) / jnp.sqrt(v + eps)

def _scatter_add(tgt, idx, src, axis=0):
    return tgt.at[idx].add(src)

def _segment_sum(src, seg, n):
    return jax.ops.segment_sum(src, seg, n)
kernel_name = 'mk_cond_resid_d2_seqx_r4_3b019e'

def setup_inputs(seed: int=0):
    np.random.seed(seed)
    _w = jnp.asarray

    def _rec_inputs():
        import jax
        import jax.numpy as jnp
        _rk = jax.random.key(seed)
        x = -7.109e-05 + 0.9999 * jax.random.normal(jax.random.fold_in(_rk, 1), (128, 64, 512), jnp.float32)
        _lenS = 64 - jax.random.randint(jax.random.fold_in(_rk, 7), (128,), 0, max(1, 64 // 4) + 1, jnp.int32)
        _lenS2 = 64 - jax.random.randint(jax.random.fold_in(_rk, 8), (128,), 0, max(1, 64 // 4) + 1, jnp.int32)
        itok_B_0_7 = jax.random.randint(jax.random.fold_in(_rk, 11), (128,), 0, 8, jnp.int32)
        itok_B_0_3 = jax.random.randint(jax.random.fold_in(_rk, 12), (128,), 0, 4, jnp.int32)
        return (x, itok_B_0_7, itok_B_0_3)
    x, itok_B_0_7, itok_B_0_3 = _rec_inputs()

    def _L0_cond_setup():
        import jax, jax.numpy as jnp
        import numpy as np
        B, C, D, T, N_SUBJECTS = (128, 64, 64, 512, 8)
        key = jax.random.key(seed)
        kx, ks, kw = jax.random.split(key, 3)
        x = jax.random.normal(kx, (B, C, T), dtype=jnp.float32)
        subjects = jax.random.randint(ks, (B,), 0, N_SUBJECTS, dtype=jnp.int64)
        weights = jax.random.normal(kw, (N_SUBJECTS, C, D), dtype=jnp.float32) * (1.0 / C ** 0.5)
        return {'x': x, 'subjects': subjects, 'weights': weights}
    _L0_cond_all = _L0_cond_setup()
    _L0_cond_in = {k: v for k, v in _L0_cond_all.items() if k in ('weights',)}
    del _L0_cond_all

    def _L1_cond_setup():
        import jax, jax.numpy as jnp
        import numpy as np
        B, S, D_IN, D_OUT, R, E = (8, 512, 512, 512, 16, 4)
        key = jax.random.key(seed)
        ks = jax.random.split(key, 7)
        x = jax.random.normal(ks[0], (B, S, D_IN), dtype=jnp.float32)
        W_base = jax.random.normal(ks[1], (D_OUT, D_IN), dtype=jnp.float32) * 0.02
        Wt = jax.random.normal(ks[2], (D_IN, D_IN), dtype=jnp.float32) * 0.02
        A = jax.random.normal(ks[3], (E, R, D_IN), dtype=jnp.float32) * 0.02
        B_w = jax.random.normal(ks[4], (E, D_OUT, R), dtype=jnp.float32) * 0.02
        Wp = jax.random.normal(ks[5], (D_OUT, D_OUT), dtype=jnp.float32) * 0.02
        scaling = jnp.ones((E,), dtype=jnp.float32)
        adapter_idx = jax.random.randint(ks[6], (B,), 0, E)
        return {'x': x, 'W_base': W_base, 'Wt': Wt, 'A': A, 'B_w': B_w, 'Wp': Wp, 'scaling': scaling, 'adapter_idx': adapter_idx}
    _L1_cond_all = _L1_cond_setup()
    _L1_cond_in = {k: v for k, v in _L1_cond_all.items() if k in ('W_base', 'Wt', 'A', 'B_w', 'Wp', 'scaling')}
    del _L1_cond_all
    return {'x': x, 'itok_B_0_7': itok_B_0_7, 'itok_B_0_3': itok_B_0_3, 'L0_cond_weights': _L0_cond_in['weights'], 'L1_cond_W_base': _L1_cond_in['W_base'], 'L1_cond_Wt': _L1_cond_in['Wt'], 'L1_cond_A': _L1_cond_in['A'], 'L1_cond_B_w': _L1_cond_in['B_w'], 'L1_cond_Wp': _L1_cond_in['Wp'], 'L1_cond_scaling': _L1_cond_in['scaling']}

def reference(x, itok_B_0_7, itok_B_0_3, L0_cond_weights, L1_cond_W_base, L1_cond_Wt, L1_cond_A, L1_cond_B_w, L1_cond_Wp, L1_cond_scaling):
    import jax
    import jax.numpy as jnp

    def _L0_cond_ref(x, subjects, weights):
        import jax, jax.numpy as jnp
        import numpy as np
        B, C, D, T, N_SUBJECTS = (128, 64, 64, 512, 8)
        w = weights[subjects]
        out = jnp.einsum('bct,bcd->bdt', x, w)
        return out

    def _L1_cond_ref(x, W_base, Wt, A, B_w, Wp, scaling, adapter_idx):
        import jax, jax.numpy as jnp
        import numpy as np
        B, S, D_IN, D_OUT, R, E = (8, 512, 512, 512, 16, 4)
        base = jnp.einsum('bsi,oi->bso', x, W_base)
        h = jnp.einsum('bsi,ji->bsj', x, Wt)
        Ab = A[adapter_idx]
        Bb = B_w[adapter_idx]
        sc = scaling[adapter_idx]
        z = jnp.einsum('bsj,brj->bsr', h, Ab)
        l = jnp.einsum('bsr,bor->bso', z, Bb)
        lora_out = jnp.einsum('bso,po->bsp', l, Wp) * sc[:, None, None]
        return base + lora_out
    x = x + _L0_cond_ref(x, itok_B_0_7, L0_cond_weights)
    x = x + _L1_cond_ref(x, L1_cond_W_base, L1_cond_Wt, L1_cond_A, L1_cond_B_w, L1_cond_Wp, L1_cond_scaling, itok_B_0_3)
    return x

_drawn_inputs = setup_inputs


def setup_inputs(seed=0):
    import zlib

    import numpy as np

    out = dict(_drawn_inputs(seed))
    spreads = {'L1_cond_scaling': (1.0, 0.6)}
    factors = {'L1_cond_Wt': 8.0,
     'L1_cond_A': 8.0,
     'L1_cond_B_w': 8.0,
     'L1_cond_Wp': 8.0,
     'L1_cond_W_base': 4.738}
    for name, (base, spread) in spreads.items():
        noise = np.random.default_rng([zlib.crc32(name.encode()), seed]).standard_normal(out[name].shape)
        drawn = base * np.exp(spread * noise) if base else spread * noise
        out[name] = jnp.asarray(drawn.astype(out[name].dtype))
    for name, factor in factors.items():
        out[name] = (out[name] * factor).astype(out[name].dtype)
    return out
```

```python
import concourse.bass as bass
from concourse import mybir
from contextlib import ExitStack


def cond_resid_kernel(nc, x, subjects, adapters, w0, wb_t, wt, a_t, b_w, wp_t, scaling, out):
    f32 = mybir.dt.float32
    f32r = mybir.dt.float32r
    i32 = mybir.dt.int32
    ALU = mybir.AluOpType
    ACT = mybir.ActivationFunctionType
    AX = mybir.AxisListType

    B, P, NT, C = x.shape
    T = NT * P
    S = w0.shape[0]
    E, R = scaling.shape[0], 16
    ER = 2 * R
    NPAIR = (B + E) // 2
    NSLOT = 2 * NPAIR
    U = 3
    NIT = NPAIR // U
    assert NPAIR % U == 0 and 2 * C == P and E * ER == P

    ctx = ExitStack()
    with ctx:
        def sb(name, shape, dt=f32):
            return ctx.enter_context(nc.sbuf_tensor(name, shape, dt))

        def sem(name):
            return ctx.enter_context(nc.semaphore(name))

        wb_sb = sb("wb_sb", [P, NT * T])
        wt_sb = sb("wt_sb", [P, NT, T])
        wp_sb = sb("wp_sb", [P, NT, T])
        a_in = sb("a_in", [P, NT, E * R])
        b_in = sb("b_in", [P, NT, E * R])
        a_dup = sb("a_dup", [P, NT, E, 2, R])
        b_dup = sb("b_dup", [P, NT, E, 2, R])
        scale_col = sb("scale_col", [P, 1])
        low_rows = sb("low_rows", [P, 1])
        sign_rows = sb("sign_rows", [P, 1])
        p_h = sb("p_h", [P, T], f32r)
        p_low = sb("p_low", [P, T])
        p_hl = sb("p_hl", [P, T], f32r)
        q_full = sb("q_full", [P, T])
        q_h = sb("q_h", [P, T], f32r)
        q_l = sb("q_l", [P, T], f32r)
        m_full = sb("m_full", [P, NT, T])
        m_h = sb("m_h", [P, E, NT, T], f32r)
        m_l = sb("m_l", [P, E, NT, T], f32r)
        w0_sb = sb("w0_sb", [P, S, C])
        w0_hl = sb("w0_hl", [P, S, 2, C], f32r)
        ident = sb("ident", [P, P])

        adapters4 = sb("adapters4", [E, B], i32)
        keys_i = sb("keys_i", [P, 2], i32)
        part_i = sb("part_i", [P, 1], i32)
        slot_i = sb("slot_i", [P, NSLOT], i32)
        part_f = sb("part_f", [P, 1])
        slot_f = sb("slot_f", [P, NSLOT])
        keys = sb("keys", [P, 4])
        ones = sb("ones", [P, P])
        ones2 = sb("ones2", [1, NSLOT])
        before = sb("before", [E, E])
        a4 = sb("a4", [E, B])
        mine = sb("mine", [E, B])
        rank = sb("rank", [E, B])
        padded_i = sb("padded_i", [E, 2], i32)
        padded = sb("padded", [E, 1])
        base = sb("base", [E, 1])
        place4 = sb("place4", [E, B])
        place = sb("place", [P, 1])
        chosen = sb("chosen", [P, NSLOT])
        unused = sb("unused", [1, NSLOT])
        unused_rank = sb("unused_rank", [1, NSLOT])
        spare_row = sb("spare_row", [1, NSLOT])
        TL = 8
        t_in = sb("t_in", [1, NIT, TL], i32)
        t_out = sb("t_out", [1, NIT, TL], i32)
        t_subject = sb("t_subject", [1, NIT, TL], i32)
        t_adapter = sb("t_adapter", [1, NPAIR + U + 3], i32)

        x_in = sb("x_in", [P, U, 2, NT, C])
        x_h = sb("x_h", [P, U, NT, 2, C], f32r)
        x_l = sb("x_l", [P, U, NT, 2, C], f32r)
        blk = sb("blk", [P, U, 2, P], f32r)
        y_h = sb("y_h", [P, U, T], f32r)
        y_l = sb("y_l", [P, U, T], f32r)
        o_sb = sb("o_sb", [P, U, T])

        ps = [ctx.enter_context(nc.psum_tensor(f"ps{i}", [P, T], f32)) for i in range(8)]
        y_ps, o_ps, m_ps = ps[0:3], ps[3:6], ps[6:8]
        p_ps, q_ps = ps[6], ps[7]
        base_ps, place_ps = ps[3], ps[4]
        rows_ps, count_ps = ps[5], ps[3]

        s_keys, s_small, s_wt, s_wp, s_wb, s_w0 = map(sem, ("s_keys", "s_small", "s_wt", "s_wp", "s_wb", "s_w0"))
        x_loaded = [sem(f"x_loaded{u}") for u in range(U)]
        stored = [sem(f"stored{u}") for u in range(U)]
        s_iota, s_mem, s_ident, s_before = map(sem, ("s_iota", "s_mem", "s_ident", "s_before"))
        s_order, s_order_pe, s_tables = map(sem, ("s_order", "s_order_pe", "s_tables"))
        s_dup, s_p, s_q, s_phq, s_pq, s_base = map(sem, ("s_dup", "s_p", "s_q", "s_phq", "s_pq", "s_base"))
        s_wsum, s_w0r, s_w0_hl, s_low = map(sem, ("s_wsum", "s_w0r", "s_w0_hl", "s_low"))
        m_made, m_summed, m_h_ready, m_l_ready = map(sem, ("m_made", "m_summed", "m_h_ready", "m_l_ready"))
        xh_ready, xl_ready = map(sem, ("xh_ready", "xl_ready"))
        y_done, yh_ready, yl_ready = map(sem, ("y_done", "yh_ready", "yl_ready"))
        blk_ready, o_done, o_copied = map(sem, ("blk_ready", "o_done", "o_copied"))

        block = ctx.enter_context(nc.Block())

        @block.sync
        def _(sp):
            sp.dma_start(adapters4[:, :], adapters.rearrange("(a n) -> a n", a=1).to_broadcast([E, B])).then_inc(s_keys, 16)
            sp.dma_start(keys_i[:, 0:1], subjects.rearrange("(n a) -> n a", a=1)).then_inc(s_keys, 16)
            sp.dma_start(keys_i[:, 1:2], adapters.rearrange("(n a) -> n a", a=1)).then_inc(s_keys, 16)
            sp.dma_start(wt_sb[:, :, :], wt.rearrange("(p c) n -> p c n", c=NT)).then_inc(s_wt, 16)
            sp.dma_start(wb_sb[:, :].rearrange("p (k o) -> p k o", k=NT), wb_t.rearrange("(k p) o -> p k o", p=P)).then_inc(s_wb, 16)

            regs = [sp.alloc_register(f"sp_row{n}") for n in range(TL)]

            def table_row(table, i, top=NSLOT - 1):
                for q in range(0, TL, 4):
                    sp.load(regs[q:q + 4], table[0:1, bass.ds(i, 1), q:q + 4].rearrange("a b c -> a (b c)"))
                return [sp.snap(regs[n], min_val=0, max_val=top) for n in range(2 * U)]

            def load_pair(u, batches):
                for half in range(2):
                    b = batches[2 * u + half]
                    sp.dma_start(x_in[:, u, half, :, :].rearrange("p k c -> p (k c)"),
                                 x[bass.ds(b, 1), :, :, :].rearrange("a p k c -> (a p) (k c)")).then_inc(x_loaded[u], 16)

            def store_pair(u, rows):
                for half in range(2):
                    b = rows[2 * u + half]
                    sp.dma_start(out[bass.ds(b, 1), :, :].rearrange("a c t -> (a c) t"),
                                 o_sb[C * half:C * half + C, u, :]).then_inc(stored[u], 16)

            sp.wait_ge(s_tables, 4)
            batches = table_row(t_in, 0, B - 1)
            for u in range(U):
                load_pair(u, batches)
            with sp.Fori(0, NIT - 1) as i:
                batches = table_row(t_in, i + 1, B - 1)
                for u in range(U):
                    sp.wait_ge(xl_ready, i * U + (u + 1))
                    load_pair(u, batches)
                rows = table_row(t_out, i)
                for u in range(U):
                    sp.wait_ge(o_copied, i * U + (u + 1))
                    store_pair(u, rows)
            rows = table_row(t_out, NIT - 1)
            for u in range(U):
                sp.wait_ge(o_copied, (NIT - 1) * U + u + 1)
                store_pair(u, rows)
            for u in range(U):
                sp.wait_ge(stored[u], 2 * 16 * NIT)

        @block.gpsimd
        def _(pool):
            nc.gpsimd.iota(part_i[:, :], [[0, 1]], base=0, channel_multiplier=1).then_inc(s_iota, 1)
            nc.gpsimd.iota(slot_i[:, :], [[1, NSLOT]], base=1, channel_multiplier=0).then_inc(s_iota, 1)
            nc.gpsimd.memset(ones[:, :], 1.0).then_inc(s_mem, 1)
            pool.wait_ge(s_mem, 1)
            nc.gpsimd.affine_select(out=before[:, :], in_=ones[0:E, 0:E], pattern=[[1, E]], compare_op=ALU.is_gt,
                                    fill=0.0, base=0, channel_multiplier=-1).then_inc(s_before, 1)
            nc.gpsimd.affine_select(out=ident[:, :], in_=ones[:, :], pattern=[[-1, P]], compare_op=ALU.is_equal,
                                    fill=0.0, base=0, channel_multiplier=1).then_inc(s_ident, 1)
            nc.gpsimd.memset(blk[:, :, :, :].bitcast(f32), 0.0).then_inc(s_mem, 1)
            pool.wait_ge(s_mem, 2)

            regs = [pool.alloc_register(f"pool_row{n}") for n in range(TL)]

            def subjects_of(i):
                for q in range(0, TL, 4):
                    pool.load(regs[q:q + 4], t_subject[0:1, bass.ds(i, 1), q:q + 4].rearrange("a b c -> a (b c)"))
                return [pool.snap(regs[n], min_val=0, max_val=S - 1) for n in range(2 * U)]

            def build(u, j, slots):
                for half in range(2):
                    rows = slice(C * half, C * half + C)
                    src = w0_hl[rows, bass.ds(slots[2 * u + half], 1), :, :].rearrange("p a b c -> p (a b) c")
                    nc.gpsimd.tensor_copy(blk[rows, u, :, rows], src).then_inc(blk_ready, 1)
                    pool.wait_ge(blk_ready, j * 2 + (half + 1))

            pool.wait_ge(s_tables, 4)
            pool.wait_ge(s_w0_hl, 2)
            slots = subjects_of(0)
            for u in range(U):
                build(u, u, slots)
            for n in range(E * NT):
                pool.wait_ge(m_h_ready, n + 1)
                nc.gpsimd.tensor_tensor(out=m_l[:, n // NT, n % NT, :], in0=m_full[:, n % NT, :],
                                        in1=m_h[:, n // NT, n % NT, :].bitcast(f32), op=ALU.subtract).then_inc(m_l_ready, 1)
            pool.wait_ge(m_l_ready, E * NT)
            with pool.Fori(1, NIT) as i:
                slots = subjects_of(i)
                for u in range(U):
                    pool.wait_ge(o_done, (i - 1) * U + (u + 1))
                    build(u, i * U + u, slots)

        @block.scalar
        def _(act):
            act.dma_start(a_in[:, :, :], a_t.rearrange("(p c) n -> p c n", c=NT)).then_inc(s_small, 16)
            act.dma_start(b_in[:, :, :], b_w.rearrange("(p c) n -> p c n", c=NT)).then_inc(s_small, 16)
            act.dma_start(scale_col[:, :], scaling.rearrange("(e a) -> e a", a=1).to_broadcast([E, ER])
                          .rearrange("e (n a) -> e n a", a=1)).then_inc(s_small, 16)
            for half in range(2):
                act.dma_start(w0_sb[C * half:C * half + C, :, :], w0.rearrange("s c d -> c s d")).then_inc(s_w0, 16)
            act.dma_start(wp_sb[:, :, :], wp_t.rearrange("(p c) n -> p c n", c=NT)).then_inc(s_wp, 16)

            act.wait_ge(s_wsum, 1)
            nc.scalar.activation(w0_hl[:, :, 0, :], w0_sb[:, :, :], ACT.Copy).then_inc(s_w0r, 1)
            act.wait_ge(s_p, 1)
            nc.scalar.activation(p_h[:, :], p_ps[:, :], ACT.Copy).then_inc(s_phq, 1)
            act.wait_ge(s_q, 1)
            act.wait_ge(s_small, 48)
            nc.scalar.activation(q_full[:, :], q_ps[:, :], ACT.Copy, scale=scale_col[:, 0:1]).then_inc(s_phq, 1)
            act.wait_ge(s_phq, 2)
            nc.scalar.activation(q_h[:, :], q_full[:, :], ACT.Copy).then_inc(s_phq, 1)
            for n in range(E * NT):
                act.wait_ge(m_summed, n + 1)
                nc.scalar.activation(m_h[:, n // NT, n % NT, :], m_full[:, n % NT, :], ACT.Copy).then_inc(m_h_ready, 1)

            def round_x(u, uses):
                act.wait_ge(x_loaded[u], uses * 32)
                nc.scalar.activation(x_h[:, u, :, :, :].rearrange("p k h c -> p h k c"), x_in[:, u, :, :, :],
                                     ACT.Copy).then_inc(xh_ready, 1)

            def round_y(u, j):
                act.wait_ge(y_done, j + 1)
                nc.scalar.activation(y_h[:, u, :], y_ps[u][:, :], ACT.Copy).then_inc(yh_ready, 1)

            def copy_out(u, j, uses):
                if uses is not None:
                    act.wait_ge(stored[u], uses * 32)
                act.wait_ge(o_done, j + 1)
                nc.scalar.activation(o_sb[:, u, :], o_ps[u][:, :], ACT.Copy).then_inc(o_copied, 1)

            for j in range(2):
                round_x(j, 1)
            round_y(0, 0)
            round_x(2, 1)
            for j in range(U):
                round_y((j + 1) % U, j + 1)
                copy_out(j, j, None)
                round_x(j, 2)
            with act.Fori(1, NIT - 1) as i:
                for u in range(U):
                    round_y((u + 1) % U, i * U + (u + 1))
                    copy_out(u, i * U + u, i)
                    round_x(u, i + 2)
            for j in range(NPAIR - U, NPAIR):
                if j + 1 < NPAIR:
                    round_y((j + 1) % U, j + 1)
                copy_out(j % U, j, NIT - 1)

        @block.vector
        def _(dve):
            chained = [0]

            def then(ins):
                chained[0] += 1
                ins.then_inc(s_order, 1)
                dve.wait_ge(s_order, chained[0])

            dve.wait_ge(s_iota, 2)
            nc.vector.tensor_copy(part_f[:, :], part_i[:, :])
            nc.vector.tensor_copy(slot_f[:, :], slot_i[:, :])
            nc.vector.tensor_copy(keys[:, 0:1], part_i[:, :])
            nc.vector.memset(keys[:, 3:4], 1.0)
            nc.vector.memset(ones2[:, :], 1.0)
            nc.vector.memset(t_adapter[:, :], 0)
            nc.vector.memset(t_in[:, :, :], 0)
            nc.vector.memset(t_out[:, :, :], 0)
            nc.vector.memset(t_subject[:, :, :], 0)
            dve.wait_ge(s_keys, 48)
            nc.vector.tensor_copy(keys[:, 1:3], keys_i[:, :])
            then(nc.vector.tensor_copy(a4[:, :], adapters4[:, :]))
            then(nc.vector.tensor_scalar(mine[:, :], a4[:, :], part_f[0:E, 0:1], None, ALU.is_equal))
            dve.wait_ge(s_mem, 1)
            then(nc.vector.tensor_tensor_scan(rank[:, :], ones[0:E, 0:B], mine[:, :], 0.0, ALU.mult, ALU.add))
            then(nc.vector.tensor_scalar(padded_i[:, 0:1], rank[:, B - 1:B], 1.0, None, ALU.add))
            then(nc.vector.tensor_scalar(padded_i[:, 1:2], padded_i[:, 0:1], -2, None, ALU.bitwise_and))
            then(nc.vector.tensor_copy(padded[:, :], padded_i[:, 1:2]))
            dve.wait_ge(s_order_pe, 1)
            then(nc.vector.tensor_copy(base[:, :], base_ps[0:E, 0:1]))
            then(nc.vector.scalar_tensor_tensor(out=place4[:, :], in0=rank[:, :], scalar=base[:, 0:1], in1=mine[:, :],
                                                op0=ALU.add, op1=ALU.mult))
            dve.wait_ge(s_order_pe, 2)
            then(nc.vector.tensor_copy(place[:, :], place_ps[:, 0:1]))
            then(nc.vector.tensor_scalar(chosen[:, :], slot_f[:, :], place[:, 0:1], None, ALU.is_equal))
            dve.wait_ge(s_order_pe, 3)

            def rows(n):
                return rows_ps[0:1, n * NSLOT:(n + 1) * NSLOT]

            def by_turn(row):
                return row.rearrange("a (i n) -> a i n", n=2 * U)

            nc.vector.tensor_copy(t_in[0:1, :, 0:2 * U], by_turn(rows(0))).then_inc(s_tables, 1)
            nc.vector.tensor_copy(t_subject[0:1, :, 0:2 * U], by_turn(rows(1))).then_inc(s_tables, 1)
            nc.vector.tensor_copy(t_adapter[0:1, 0:NPAIR], rows(2).rearrange("a (i n) -> a i n", n=2)[:, :, 0]).then_inc(s_tables, 1)
            then(nc.vector.tensor_scalar(unused[:, :], count_ps[0:1, 0:NSLOT], -1.0, 1.0, ALU.mult, ALU.add))
            then(nc.vector.tensor_tensor_scan(unused_rank[:, :], ones2[0:1, 0:NSLOT], unused[:, :], 0.0, ALU.mult, ALU.add))
            then(nc.vector.scalar_tensor_tensor(out=spare_row[:, :], in0=unused_rank[:, :], scalar=float(B - 1), in1=unused[:, :],
                                                op0=ALU.add, op1=ALU.mult))
            nc.vector.tensor_tensor(out=t_out[0:1, :, 0:2 * U], in0=by_turn(rows(0)), in1=by_turn(spare_row[0:1, :]),
                                    op=ALU.add).then_inc(s_tables, 1)

            dve.wait_ge(s_small, 48)
            for src, dst in ((a_in, a_dup), (b_in, b_dup)):
                for n in range(2):
                    last = nc.vector.tensor_copy(dst[:, :, :, n, :], src[:, :, :].rearrange("p c (e r) -> p c e r", r=R))
            last.then_inc(s_dup, 1)
            dve.wait_ge(s_ident, 1)
            dve.wait_ge(s_w0, 32)
            for half in range(2):
                r = slice(C * half, C * half + C)
                eye = ident[r, r].rearrange("p (a c) -> p a c", a=1).to_broadcast([C, S, C])
                last = nc.vector.tensor_tensor(out=w0_sb[r, :, :], in0=w0_sb[r, :, :], in1=eye, op=ALU.add)
            last.then_inc(s_wsum, 1)
            dve.wait_ge(s_w0r, 1)
            nc.vector.tensor_tensor(out=w0_hl[:, :, 1, :], in0=w0_sb[:, :, :], in1=w0_hl[:, :, 0, :].bitcast(f32),
                                    op=ALU.subtract).then_inc(s_w0_hl, 2)
            then(nc.vector.tensor_reduce(out=low_rows[:, :], in_=ident[:, :].rearrange("p (e n r) -> p e n r", e=E, n=2)[:, :, 1, :],
                                         axis=AX.XY, op=ALU.add))
            then(nc.vector.tensor_scalar(sign_rows[:, :], low_rows[:, :], -2.0, 1.0, ALU.mult, ALU.add))
            dve.wait_ge(s_wb, 16)
            for k in range(NT):
                o = k * T + k * P
                last = nc.vector.tensor_tensor(out=wb_sb[:, o:o + P], in0=wb_sb[:, o:o + P], in1=ident[:, :], op=ALU.add)
            last.then_inc(s_base, 1)
            dve.wait_ge(s_phq, 1)
            then(nc.vector.tensor_scalar(p_low[:, :], p_ps[:, :], low_rows[:, 0:1], None, ALU.mult))
            nc.vector.scalar_tensor_tensor(out=p_hl[:, :], in0=p_h[:, :].bitcast(f32), scalar=sign_rows[:, 0:1], in1=p_low[:, :],
                                           op0=ALU.mult, op1=ALU.add)
            dve.wait_ge(s_phq, 3)
            nc.vector.tensor_tensor(out=q_l[:, :], in0=q_full[:, :], in1=q_h[:, :].bitcast(f32), op=ALU.subtract).then_inc(s_pq, 1)
            dve.wait_ge(s_base, 1)
            for n in range(E * NT):
                dve.wait_ge(m_made, n + 1)
                if n >= NT:
                    dve.wait_ge(m_l_ready, n - NT + 1)
                nc.vector.tensor_tensor(out=m_full[:, n % NT, :], in0=m_ps[n % 2][:, :], in1=wb_sb[:, (n % NT) * T:(n % NT + 1) * T],
                                        op=ALU.add).then_inc(m_summed, 1)

            def rest_of_x(u, j):
                dve.wait_ge(xh_ready, j + 1)
                nc.vector.tensor_tensor(out=x_l[:, u, :, :, :].rearrange("p k h c -> p h k c"), in0=x_in[:, u, :, :, :],
                                        in1=x_h[:, u, :, :, :].rearrange("p k h c -> p h k c").bitcast(f32),
                                        op=ALU.subtract).then_inc(xl_ready, 1)

            def rest_of_y(u, j):
                dve.wait_ge(yh_ready, j + 1)
                nc.vector.tensor_tensor(out=y_l[:, u, :], in0=y_ps[u][:, :], in1=y_h[:, u, :].bitcast(f32),
                                        op=ALU.subtract).then_inc(yl_ready, 1)

            for j in range(2):
                rest_of_x(j, j)
            with dve.Fori(0, NIT - 1) as i:
                for u in range(U):
                    rest_of_y(u, i * U + u)
                    rest_of_x((u + 2) % U, i * U + (u + 2))
            for j in range(NPAIR - U, NPAIR):
                rest_of_y(j % U, j)
                if j + 2 < NPAIR:
                    rest_of_x((j + 2) % U, j + 2)

        @block.tensor
        def _(pe):
            mm = nc.tensor.matmul
            pe.wait_ge(s_before, 1)
            pe.wait_ge(s_order, 6)
            mm(base_ps[0:E, 0:1], before[:, :], padded[:, :], start=True, stop=True).then_inc(s_order_pe, 1)
            pe.wait_ge(s_order, 8)
            mm(place_ps[:, 0:1], place4[:, :], ones[0:E, 0:1], start=True, stop=True).then_inc(s_order_pe, 1)
            pe.wait_ge(s_order, 10)
            for n in range(3):
                mm(rows_ps[0:1, n * NSLOT:(n + 1) * NSLOT], keys[:, n:n + 1], chosen[:, :], start=True, stop=True)
            mm(count_ps[0:1, 0:NSLOT], keys[:, 3:4], chosen[:, :], start=True, stop=True).then_inc(s_order_pe, 1)

            pe.wait_ge(s_dup, 1)
            pe.wait_ge(s_wt, 16)
            for c in range(NT):
                last = mm(p_ps[:, :], a_dup[:, c, :, :, :].rearrange("p e n r -> p (e n r)"), wt_sb[:, c, :],
                          start=c == 0, stop=c == NT - 1)
            last.then_inc(s_p, 1)
            pe.wait_ge(s_wp, 16)
            for c in range(NT):
                last = mm(q_ps[:, :], b_dup[:, c, :, :, :].rearrange("p e n r -> p (e n r)"), wp_sb[:, c, :],
                          start=c == 0, stop=c == NT - 1)
            last.then_inc(s_q, 1)
            pe.wait_ge(s_pq, 1)
            for n in range(E * NT):
                if n >= 2:
                    pe.wait_ge(m_summed, n - 1)
                r = slice(ER * (n // NT), ER * (n // NT) + ER)
                for q in (q_h, q_l):
                    last = mm(m_ps[n % 2][:, :], p_hl[r, (n % NT) * P:(n % NT + 1) * P], q[r, :],
                              start=q is q_h, stop=q is q_l)
                last.then_inc(m_made, 1)

            regs = [pe.alloc_register(f"pe_row{n}") for n in range(4)]

            def adapters_of(first):
                pe.load(regs, t_adapter[0:1, bass.ds(first, 4)])
                return [pe.snap(regs[n], min_val=0, max_val=E - 1) for n in range(4)]

            def times_m(u, j, e):
                pe.wait_ge(xl_ready, j + 1)
                for k in range(NT):
                    for n, (xs, ms) in enumerate(((x_h, m_h), (x_h, m_l), (x_l, m_h))):
                        last = mm(y_ps[u][:, :], xs[:, u, k, :, :].rearrange("p h c -> p (h c)"), ms[:, bass.ds(e, 1), k, :].rearrange("p a n -> p (a n)"),
                                  start=k == 0 and n == 0, stop=k == NT - 1 and n == 2)
                last.then_inc(y_done, 1)

            def times_w(u, j, first=False):
                pe.wait_ge(yl_ready, j + 1)
                pe.wait_ge(blk_ready, j * 2 + 2)
                if not first:
                    pe.wait_ge(o_copied, j + (1 - U))
                for n, (w, ys) in enumerate(((0, y_h), (1, y_h), (0, y_l))):
                    last = mm(o_ps[u][:, :], blk[:, u, w, :], ys[:, u, :], start=n == 0, stop=n == 2)
                last.then_inc(o_done, 1)

            pe.wait_ge(m_l_ready, E * NT)
            pe.wait_ge(s_tables, 4)
            es = adapters_of(0)
            for j in range(U):
                times_m(j, j, es[j])
                if j > 0:
                    times_w(j - 1, j - 1, True)
            times_m(0, U, es[U])
            times_w(U - 1, U - 1, True)
            with pe.Fori(1, NIT - 1) as i:
                es = adapters_of(i * U + 1)
                for u in range(U):
                    times_m((u + 1) % U, i * U + (u + 1), es[u])
                    times_w(u, i * U + u)
            es = adapters_of(NPAIR - U + 1)
            for j in range(NPAIR - U, NPAIR):
                if j + 1 < NPAIR:
                    times_m((j + 1) % U, j + 1, es[j - (NPAIR - U)])
                times_w(j % U, j)


def kernel(x, itok_B_0_7, itok_B_0_3, L0_cond_weights, L1_cond_W_base, L1_cond_Wt, L1_cond_A, L1_cond_B_w,
           L1_cond_Wp, L1_cond_scaling):
    import numpy as np
    import concourse.bacc as bacc
    from concourse import mybir as mb
    from concourse.bass_utils import run_bass_kernel_spmd as run

    batches, channels, T = x.shape
    E, R, D = L1_cond_A.shape
    P = 128
    K = T // P
    laid = {
        "x": np.asarray(x).reshape(batches, channels, K, P).transpose(0, 3, 2, 1),
        "subjects": itok_B_0_7,
        "adapters": itok_B_0_3,
        "w0": L0_cond_weights,
        "wb_t": np.asarray(L1_cond_W_base).T,
        "wt": L1_cond_Wt,
        "a_t": np.asarray(L1_cond_A).reshape(E * R, D).T,
        "b_w": np.asarray(L1_cond_B_w).transpose(1, 0, 2).reshape(D, E * R),
        "wp_t": np.asarray(L1_cond_Wp).T,
        "scaling": L1_cond_scaling,
    }
    nc = bacc.Bacc("TRN2", target_bir_lowering=False, num_devices=1)
    arrays, args = {}, []
    for name, a in laid.items():
        a = np.ascontiguousarray(a)
        arrays[f"in_{name}"] = a
        args.append(nc.dram_tensor(f"in_{name}", a.shape, mb.dt.from_np(a.dtype), kind="ExternalInput").ap())
    out = nc.dram_tensor("out", (batches + E, channels, T), mb.dt.float32, kind="ExternalOutput").ap()
    cond_resid_kernel(nc, *args, out)
    r = run(nc, [arrays], core_ids=[0])
    return r.results[0]["out"][:batches]
```
